# Optimizing a Trainium2 kernel written in Bass

```python
import numpy as np
import jax
import jax.numpy as jnp

def _softmax(x, axis=-1):
    return jax.nn.softmax(x, axis=axis)
def _gelu(x):
    return jax.nn.gelu(x, approximate=True)
def _silu(x):
    return jax.nn.silu(x)
def _sigmoid(x):
    return jax.nn.sigmoid(x)
def _layernorm(x, axis=-1, eps=1e-5):
    m = jnp.mean(x, axis=axis, keepdims=True)
    v = jnp.var(x, axis=axis, keepdims=True)
    return (x - m) / jnp.sqrt(v + eps)
def _scatter_add(tgt, idx, src, axis=0):
    return tgt.at[idx].add(src)
def _segment_sum(src, seg, n):
    return jax.ops.segment_sum(src, seg, n)

kernel_name = 'mk_adj_preln_d1_adj_256_27b13c'

def setup_inputs(seed: int = 0):
    np.random.seed(seed)
    _w = jnp.asarray
    def _rec_inputs():
        import jax
        import jax.numpy as jnp
        _gk = jax.random.key(seed)
        x = -0.0005207 + 1.001 * jax.random.normal(jax.random.fold_in(_gk, 1), (8192, 256), jnp.float32)
        _w = (1.0 + jnp.arange(8192, dtype=jnp.float32)) ** -0.5
        _w = _w / _w.mean()
        _pij = jnp.clip(0.000488281 * _w[:, None] * _w[None, :], 0.0, 1.0)
        _a = jax.random.uniform(jax.random.fold_in(_gk, 2), (8192, 8192)) < _pij
        adj = _a.astype(jnp.int32)
        return x, adj
    x, adj = _rec_inputs()
    def _L0_gnn_setup():
        import jax, jax.numpy as jnp
        import numpy as np
        KEEP_RATIO = 0.5
        TEMP = 1.0
        NEG_BIG = -9000000000000000.0
        N_NODE = 8192
        FEA_DIM = 256
        HID_DIM = 128
        key = jax.random.key(seed)
        ks = jax.random.split(key, 7)
        features = jax.random.normal(ks[0], (N_NODE, FEA_DIM), dtype=jnp.float32)
        adj = jax.random.randint(ks[1], (N_NODE, N_NODE), 0, 2, dtype=jnp.int32)
        W1 = jax.random.normal(ks[2], (HID_DIM, FEA_DIM), dtype=jnp.float32) * 0.001
        b1 = jax.random.normal(ks[3], (HID_DIM,), dtype=jnp.float32) * 0.001
        W2 = jax.random.normal(ks[4], (HID_DIM, FEA_DIM), dtype=jnp.float32) * 0.001
        Ww = jax.random.normal(ks[5], (1, HID_DIM), dtype=jnp.float32) * 0.001
        bw = jax.random.normal(ks[6], (1,), dtype=jnp.float32) * 0.001
        return {'features': features, 'adj': adj, 'W1': W1, 'b1': b1, 'W2': W2, 'Ww': Ww, 'bw': bw}
    _L0_gnn_all = _L0_gnn_setup()
    _L0_gnn_in = {k: v for k, v in _L0_gnn_all.items() if k in ('W1', 'b1', 'W2', 'Ww', 'bw', )}
    del _L0_gnn_all

    return {
        "x": x,
        "adj": adj,
        "L0_gnn_W1": _L0_gnn_in["W1"],
        "L0_gnn_b1": _L0_gnn_in["b1"],
        "L0_gnn_W2": _L0_gnn_in["W2"],
        "L0_gnn_Ww": _L0_gnn_in["Ww"],
        "L0_gnn_bw": _L0_gnn_in["bw"],
    }

def reference(x, adj, L0_gnn_W1, L0_gnn_b1, L0_gnn_W2, L0_gnn_Ww, L0_gnn_bw):
    import jax
    import jax.numpy as jnp
    def _L0_gnn_ref(features, adj, W1, b1, W2, Ww, bw):
        import jax, jax.numpy as jnp
        import numpy as np
        KEEP_RATIO = 0.5
        TEMP = 1.0
        NEG_BIG = -9000000000000000.0
        N_NODE = 8192
        FEA_DIM = 256
        HID_DIM = 128
        s1 = features @ W1.T + b1
        s2 = features @ W2.T
        w = Ww[0]
        u = s1 @ w + bw[0]
        v = s2 @ w
        raw_att = u[:, None] + v[None, :]
        att = jnp.where(adj > 0, raw_att, NEG_BIG) * TEMP
        att = jax.nn.softmax(att, axis=1)
        prop_fea = att @ features
        adj_num = jnp.sum(adj, axis=1)
        adj_mask = (adj_num > 0).astype(features.dtype)[:, None]
        prop_fea = adj_mask * prop_fea + (1.0 - adj_mask) * features
        out = (1.0 - KEEP_RATIO) * prop_fea + KEEP_RATIO * features
        return out

    h = jnp.maximum(_layernorm(x, axis=-1), 0.0)
    x = x + _L0_gnn_ref(h, adj, L0_gnn_W1, L0_gnn_b1, L0_gnn_W2, L0_gnn_Ww, L0_gnn_bw)
    return x


_drawn_inputs = setup_inputs


def setup_inputs(seed=0):
    import zlib

    import numpy as np

    out = dict(_drawn_inputs(seed))
    spreads = {}
    factors = {}
    for name, (base, spread) in spreads.items():
        noise = np.random.default_rng([zlib.crc32(name.encode()), seed]).standard_normal(out[name].shape)
        drawn = base * np.exp(spread * noise) if base else spread * noise
        out[name] = jnp.asarray(drawn.astype(out[name].dtype))
    for name, factor in factors.items():
        out[name] = (out[name] * factor).astype(out[name].dtype)
    return out
```

```python
import concourse.bass as bass
from concourse import mybir
from contextlib import ExitStack

P = 128
EPS = 1e-5
NEG_BIG = -9000000000000000.0
KEEP = 0.5
R_MAX = 2.75
LOG_SCALE = 7.624618986159398
TINY = 1e-30
BANKS = 8
PAIR = 2
SLOTS = 4
QUAD = 4


def fast_program(nc, x, adj_tiles, w2, ww, out, flag):
    f32, f16, i32 = mybir.dt.float32, mybir.dt.float16, mybir.dt.int32
    ALU, ACT = mybir.AluOpType, mybir.ActivationFunctionType
    N, F = x.shape
    HID = w2.shape[0]
    T = N // P
    CHUNKS = T // BANKS
    BLOCKS = T // (PAIR * SLOTS)
    TURNS = CHUNKS * BLOCKS
    C = F + 1
    CP = C + 1
    assert PAIR * SLOTS == 2 * QUAD == BANKS and N % (P * BANKS) == 0 and BLOCKS >= 2

    x_tiles = x.rearrange("(p t) f -> p t f", p=P)
    out_tiles = out.rearrange("(p t) f -> p t f", p=P)

    with ExitStack() as ctx:
        def sb(name, shape, dt):
            return ctx.enter_context(nc.sbuf_tensor(name, shape, dt))

        def sem(name):
            return ctx.enter_context(nc.semaphore(name))

        adj_sb = sb("adj_sb", [P, SLOTS, PAIR * BANKS * P], i32)
        mask = sb("mask", [P, SLOTS, PAIR * BANKS * P], f16)
        mask_tiles = mask[:, :, :].rearrange("p s (t k q) -> p s t k q", t=PAIR, k=BANKS)
        g_hi = sb("g_hi", [P, T, CP], f16)
        g_lo = sb("g_lo", [P, T, CP], f16)
        x_all = sb("x_all", [P, T, F], f32)
        h1 = sb("h1", [P, 2, QUAD, CP], f32)
        acc = sb("acc", [P, BANKS, CP], f32)
        h_rows = sb("h_rows", [P, BANKS, F], f32)
        w2_sb = sb("w2_sb", [HID, F], f32)
        w_col = sb("w_col", [HID, 1], f32)
        w_wide = sb("w_wide", [HID, P], f32)
        a2 = sb("a2", [P, F], f32)
        norm2 = sb("norm2", [P, 1], f32)
        r_squared = sb("r_squared", [P, 1], f32)
        bound = sb("bound", [P, 1], f32)
        exp_bias = sb("exp_bias", [P, 1], f32)
        half_power = sb("half_power", [P, 1], f32)
        neg_half_power = sb("neg_half_power", [P, QUAD], f32)
        stats = sb("stats", [P, QUAD, 6], f32)
        mean_var = sb("mean_var", [P, 2, QUAD, 2], f32)
        var_eps = sb("var_eps", [P, 2, QUAD], f32)
        neg_mean = sb("neg_mean", [P, 2, QUAD], f32)
        rstd = sb("rstd", [P, T], f32)
        shift = sb("shift", [P, T], f32)
        v = sb("v", [P, 2, QUAD], f32)
        e = sb("e", [P, 2, QUAD], f32)
        floor_den = sb("floor_den", [P, BANKS], f32)
        inv_den = sb("inv_den", [P, BANKS], f32)
        prop_scale = sb("prop_scale", [P, BANKS], f32)
        empty_half = sb("empty_half", [P, BANKS], f32)
        h_scale = sb("h_scale", [P, BANKS], f32)
        h_shift = sb("h_shift", [P, BANKS], f32)
        ps = ctx.enter_context(nc.psum_tensor("ps", [P, BANKS, 512], f32))

        w_loaded = sem("w_loaded")
        x_full = [sem("x_full_even"), sem("x_full_odd")]
        adj_full = [sem(f"adj_full{i}") for i in range(SLOTS)]
        mask_ready = sem("mask_ready")
        mask_free = sem("mask_free")
        w_cleared = sem("w_cleared")
        w_wide_ready = sem("w_wide_ready")
        a2_in_psum = sem("a2_in_psum")
        a2_ready = sem("a2_ready")
        norm2_ready = sem("norm2_ready")
        r_squared_ready = sem("r_squared_ready")
        flag_ready = sem("flag_ready")
        powers_ready = sem("powers_ready")
        bound_ready = sem("bound_ready")
        exp_bias_ready = sem("exp_bias_ready")
        ones_ready = sem("ones_ready")
        bn_stats_done = sem("bn_stats_done")
        wait_passed = sem("wait_passed")
        mean_var_done = sem("mean_var_done")
        var_eps_ready = sem("var_eps_ready")
        neg_mean_ready = sem("neg_mean_ready")
        rstd_ready = sem("rstd_ready")
        shift_ready = sem("shift_ready")
        h_ready = sem("h_ready")
        v_ready = sem("v_ready")
        e_ready = sem("e_ready")
        g_hi_ready = sem("g_hi_ready")
        g_ready = sem("g_ready")
        acc_done = sem("acc_done")
        bank_read = sem("bank_read")
        den_ready = sem("den_ready")
        inv_den_ready = sem("inv_den_ready")
        empty_ready = sem("empty_ready")
        prop_scale_ready = sem("prop_scale_ready")
        h_scale_ready = sem("h_scale_ready")
        h_rows_ready = sem("h_rows_ready")
        prop_added = sem("prop_added")
        out_ready = sem("out_ready")
        out_stored = sem("out_stored")

        block = ctx.enter_context(nc.Block())

        @block.sync
        def _(sp):
            def load_adjacency(turn, slot):
                n = turn * SLOTS + slot
                sp.dma_start(adj_sb[:, slot, :], adj_tiles[:, bass.ds(n, 1), :]).then_inc(adj_full[slot], 16)

            sp.dma_start(w_col[:, :], ww.rearrange("o h -> h o")).then_inc(w_loaded, 16)
            sp.dma_start(w2_sb[:, :], w2).then_inc(w_loaded, 16)
            for slot in range(SLOTS):
                load_adjacency(0, slot)
            with sp.Fori(1, TURNS) as turn:
                for slot in range(SLOTS):
                    sp.wait_ge(mask_ready, turn * SLOTS + slot - (SLOTS - 1))
                    load_adjacency(turn, slot)

        @block.gpsimd
        def _(pool):
            pool.memset(half_power[:, :], 0.5).then_inc(powers_ready, 1)
            pool.memset(neg_half_power[:, :], -0.5).then_inc(powers_ready, 1)
            pool.wait_ge(powers_ready, 2)
            pool.wait_ge(r_squared_ready, 1)
            pool.tensor_tensor(bound[:, :], r_squared[:, :], half_power[:, :], ALU.pow).then_inc(bound_ready, 1)
            pool.wait_ge(bound_ready, 1)
            pool.tensor_scalar(exp_bias[:, :], bound[:, :], -1.0, LOG_SCALE, ALU.mult, ALU.add).then_inc(exp_bias_ready, 1)
            with pool.Fori(0, BLOCKS) as blk:
                for half in range(2):
                    quad = blk * 2 + half
                    own = bass.ds(quad * QUAD, QUAD)
                    pool.wait_ge(var_eps_ready, quad + 1)
                    pool.tensor_tensor(rstd[:, own], var_eps[:, half, :], neg_half_power[:, :], ALU.pow).then_inc(rstd_ready, 1)
                    pool.wait_ge(neg_mean_ready, quad + 1)
                    pool.wait_ge(rstd_ready, quad + 1)
                    pool.tensor_tensor(shift[:, own], neg_mean[:, half, :], rstd[:, own], ALU.mult).then_inc(shift_ready, 1)

        @block.vector
        def _(dve):
            def statistics(quad, half):
                dve.wait_ge(x_full[half], (quad - half) * 8 + 16)
                for t in range(QUAD):
                    row = x_all[:, bass.ds(quad * QUAD + t, 1), :].rearrange("p o f -> p (o f)")
                    dve.bn_stats(stats[:, t, :], row).then_inc(bn_stats_done, 1)
                dve.wait_ge(bn_stats_done, quad * QUAD + QUAD)
                dve.sem_inc(wait_passed, 1)
                for t in range(QUAD):
                    dve.bn_aggr(mean_var[:, half, t, :], stats[:, t, :]).then_inc(mean_var_done, 1)
                dve.wait_ge(mean_var_done, quad * QUAD + QUAD)
                dve.tensor_scalar(var_eps[:, half, :], mean_var[:, half, :, 1], EPS, None, ALU.add).then_inc(var_eps_ready, 1)
                dve.tensor_scalar(neg_mean[:, half, :], mean_var[:, half, :, 0], -1.0, None, ALU.mult).then_inc(neg_mean_ready, 1)

            def make_mask(turn, slot):
                dve.wait_ge(adj_full[slot], turn * 16 + 16)
                dve.wait_ge(mask_free, turn * SLOTS + slot + 1)
                dve.tensor_scalar(mask[:, slot, :], adj_sb[:, slot, :], 0.0, None, ALU.is_gt)\
                   .then_inc(mask_ready, 1)

            def logits(quad, half):
                dve.wait_ge(h_ready, quad * QUAD + QUAD)
                for t in range(QUAD):
                    dve.scalar_tensor_tensor(out=h_rows[:, half * QUAD + t, :], in0=h1[:, half, t, 0:F], scalar=1.0, in1=a2[:, :],
                                             op0=ALU.mult, op1=ALU.mult, accum_out=v[:, half, t:t + 1])\
                       .then_inc(v_ready, 1)

            def low_parts(quad, half):
                dve.wait_ge(g_hi_ready, quad * QUAD + QUAD)
                for t in range(QUAD):
                    own = bass.ds(quad * QUAD + t, 1)
                    dve.scalar_tensor_tensor(
                        out=g_lo[:, own, 0:C].rearrange("p o c -> p (o c)"), in0=h1[:, half, t, 0:C],
                        scalar=e[:, half, t:t + 1], in1=g_hi[:, own, 0:C].rearrange("p o c -> p (o c)"),
                        op0=ALU.mult, op1=ALU.subtract).then_inc(g_ready, 1)

            def first_chunk(blk, more):
                for half in range(2):
                    quad = blk * 2 + half
                    if half == 0 or more:
                        statistics(quad + 1, 1 - half)
                    logits(quad, half)
                    make_mask(blk, 2 * half)
                    low_parts(quad, half)
                    make_mask(blk, 2 * half + 1)

            def finish_rows(chunk):
                own = bass.ds(chunk * BANKS, BANKS)
                dve.wait_ge(bank_read, chunk * BANKS + 2 * BANKS)
                dve.tensor_scalar(floor_den[:, :], acc[:, :, F], TINY, None, ALU.max).then_inc(den_ready, 1)
                dve.tensor_scalar(empty_half[:, :], acc[:, :, F], 0.0, KEEP, ALU.is_le, ALU.mult).then_inc(empty_ready, 1)
                dve.wait_ge(den_ready, chunk + 1)
                dve.reciprocal(inv_den[:, :], floor_den[:, :]).then_inc(inv_den_ready, 1)
                dve.wait_ge(empty_ready, chunk + 1)
                dve.scalar_tensor_tensor(out=h_scale[:, :], in0=empty_half[:, :], scalar=KEEP, in1=rstd[:, own],
                                         op0=ALU.add, op1=ALU.mult).then_inc(h_scale_ready, 1)
                dve.scalar_tensor_tensor(out=h_shift[:, :], in0=empty_half[:, :], scalar=KEEP, in1=shift[:, own],
                                         op0=ALU.add, op1=ALU.mult).then_inc(h_scale_ready, 1)
                dve.wait_ge(inv_den_ready, chunk + 1)
                dve.tensor_scalar(prop_scale[:, :], inv_den[:, :], 1.0 - KEEP, None, ALU.mult).then_inc(prop_scale_ready, 1)
                dve.wait_ge(prop_scale_ready, chunk + 1)
                for k in range(BANKS):
                    row = x_all[:, bass.ds(chunk * BANKS + k, 1), :].rearrange("p o f -> p (o f)")
                    dve.scalar_tensor_tensor(out=acc[:, k, 0:F], in0=acc[:, k, 0:F], scalar=prop_scale[:, k:k + 1],
                                             in1=row, op0=ALU.mult, op1=ALU.add).then_inc(prop_added, 1)
                dve.wait_ge(prop_added, chunk * BANKS + BANKS)
                dve.wait_ge(h_rows_ready, chunk * BANKS + BANKS)
                dve.tensor_tensor(h_rows[:, :, :], acc[:, :, 0:F], h_rows[:, :, :], ALU.add).then_inc(out_ready, 1)

            dve.memset(w_wide[:, :], 1.0).then_inc(w_cleared, 1)
            dve.memset(h1[:, :, :, F:CP], 1.0).then_inc(ones_ready, 1)
            dve.wait_ge(w_loaded, 32)
            dve.wait_ge(w_cleared, 1)
            dve.tensor_scalar(w_wide[:, :], w_wide[:, :], w_col[:, 0:1], None, ALU.mult).then_inc(w_wide_ready, 1)
            dve.wait_ge(a2_in_psum, 1)
            dve.tensor_copy(a2[:, :], ps[:, 0, 0:F]).then_inc(a2_ready, 1)
            dve.wait_ge(a2_ready, 1)
            dve.sem_inc(bank_read, BANKS)
            dve.scalar_tensor_tensor(out=acc[:, 0, 0:F], in0=a2[:, :], scalar=1.0, in1=a2[:, :], op0=ALU.mult,
                                     op1=ALU.mult, accum_out=norm2[:, 0:1]).then_inc(norm2_ready, 1)
            dve.wait_ge(norm2_ready, 1)
            dve.tensor_scalar(r_squared[:, :], norm2[:, :], float(F), None, ALU.mult).then_inc(r_squared_ready, 1)
            dve.tensor_scalar(flag[0:1, 0:1], norm2[0:1, :], R_MAX * R_MAX / F, None, ALU.is_gt).then_inc(flag_ready, 1)

            statistics(0, 0)
            with dve.Fori(0, BLOCKS - 1) as blk:
                first_chunk(blk, True)
            first_chunk(BLOCKS - 1, False)
            with dve.Fori(1, CHUNKS) as chunk:
                for slot in range(SLOTS):
                    make_mask(chunk * BLOCKS, slot)
                finish_rows(chunk - 1)
                with dve.Fori(1, BLOCKS) as blk:
                    for slot in range(SLOTS):
                        make_mask(chunk * BLOCKS + blk, slot)
            finish_rows(CHUNKS - 1)

        @block.scalar
        def _(act):
            def load_x(quad, half):
                act.dma_start(x_all[:, bass.ds(quad * QUAD, QUAD), :], x_tiles[:, bass.ds(quad * QUAD, QUAD), :])\
                   .then_inc(x_full[half], 16)

            def make_g(blk, more):
                for half in range(2):
                    quad = blk * 2 + half
                    act.wait_ge(shift_ready, quad + 1)
                    if more:
                        load_x(quad + 2, half)
                    for t in range(QUAD):
                        at = quad * QUAD + t
                        row = x_all[:, bass.ds(at, 1), :].rearrange("p o f -> p (o f)")
                        nc.scalar.activation(h1[:, half, t, 0:F], row, ACT.Relu, bias=shift[:, bass.ds(at, 1)],
                                             scale=rstd[:, bass.ds(at, 1)]).then_inc(h_ready, 1)
                    act.wait_ge(exp_bias_ready, 1)
                    act.wait_ge(v_ready, quad * QUAD + QUAD)
                    nc.scalar.activation(e[:, half, :], v[:, half, :], ACT.Exp, bias=exp_bias[:, 0:1]).then_inc(e_ready, 1)
                    act.wait_ge(ones_ready, 1)
                    act.wait_ge(e_ready, quad + 1)
                    act.wait_ge(h_ready, quad * QUAD + QUAD)
                    for t in range(QUAD):
                        own = bass.ds(quad * QUAD + t, 1)
                        nc.scalar.activation(g_hi[:, own, 0:C].rearrange("p o c -> p (o c)"), h1[:, half, t, 0:C],
                                             ACT.Copy, scale=e[:, half, t:t + 1]).then_inc(g_hi_ready, 1)

            load_x(0, 0)
            load_x(1, 1)
            with act.Fori(0, BLOCKS - 1) as blk:
                make_g(blk, True)
            make_g(BLOCKS - 1, False)
            with act.Fori(0, CHUNKS) as chunk:
                for k in range(BANKS):
                    if k < BANKS - 1:
                        act.wait_ge(acc_done, chunk * (BANKS - 1) + k + 1)
                    else:
                        act.wait_ge(mask_free, (chunk + 1) * (BLOCKS * SLOTS) + SLOTS)
                    nc.scalar.activation(acc[:, k, 0:C], ps[:, k, 0:C], ACT.Copy).then_inc(bank_read, 1)
                act.wait_ge(h_scale_ready, chunk * 2 + 2)
                act.wait_ge(out_stored, chunk * 16)
                for k in range(BANKS):
                    row = x_all[:, bass.ds(chunk * BANKS + k, 1), :].rearrange("p o f -> p (o f)")
                    nc.scalar.activation(h_rows[:, k, :], row, ACT.Relu, bias=h_shift[:, k:k + 1],
                                         scale=h_scale[:, k:k + 1]).then_inc(h_rows_ready, 1)
                act.wait_ge(out_ready, chunk + 1)
                act.dma_start(out_tiles[:, bass.ds(chunk * BANKS, BANKS), :], h_rows[:, :, :]).then_inc(out_stored, 16)
            act.wait_ge(out_stored, CHUNKS * 16)
            act.wait_ge(flag_ready, 1)

        @block.tensor
        def _(pe):
            def product(chunk, blk, first, last):
                for slot in range(SLOTS):
                    pe.wait_ge(mask_ready, (chunk * BLOCKS + blk) * SLOTS + slot + 1)
                    pe.wait_ge(g_ready, (blk * SLOTS + slot + 1) * PAIR)
                    for k in range(BANKS):
                        if first and slot == 0:
                            pe.wait_ge(bank_read, chunk * BANKS + k + 1)
                        for t in range(PAIR):
                            tile = bass.ds(blk * (SLOTS * PAIR) + slot * PAIR + t, 1)
                            begins = first and slot == 0 and t == 0
                            ends = last and slot == SLOTS - 1 and t == PAIR - 1
                            nc.tensor.matmul(ps[:, k, 0:C], mask_tiles[:, slot, t, k, :],
                                             g_hi[:, tile, 0:C].rearrange("p o c -> p (o c)"), start=begins, stop=False)
                            done = nc.tensor.matmul(ps[:, k, 0:C], mask_tiles[:, slot, t, k, :],
                                                    g_lo[:, tile, 0:C].rearrange("p o c -> p (o c)"), start=False, stop=ends)
                            if k == BANKS - 1 and t == PAIR - 1:
                                done.then_inc(mask_free, 1)
                            elif ends:
                                done.then_inc(acc_done, 1)

            pe.sem_inc(mask_free, SLOTS)
            pe.wait_ge(w_wide_ready, 1)
            nc.tensor.matmul(ps[:, 0, 0:F], w_wide[:, :], w2_sb[:, :], start=True, stop=True).then_inc(a2_in_psum, 1)
            with pe.Fori(0, CHUNKS) as chunk:
                product(chunk, 0, True, False)
                if BLOCKS > 2:
                    with pe.Fori(1, BLOCKS - 1) as blk:
                        product(chunk, blk, False, False)
                product(chunk, BLOCKS - 1, False, True)


def general_program(nc, x, adj, w1, b1, w2, ww, bw, v_row, out):
    f32, i32 = mybir.dt.float32, mybir.dt.int32
    ALU, ACT, AX = mybir.AluOpType, mybir.ActivationFunctionType, mybir.AxisListType
    N, F = x.shape
    HID = w2.shape[0]
    B = N // P

    x_tiles = x.rearrange("(b p) f -> p b f", p=P)
    out_tiles = out.rearrange("(b p) f -> p b f", p=P)
    adj_tiles = adj.rearrange("(b p) n -> p b n", p=P)

    with ExitStack() as ctx:
        def sb(name, shape, dt):
            return ctx.enter_context(nc.sbuf_tensor(name, shape, dt))

        def pb(name, shape):
            return ctx.enter_context(nc.psum_tensor(name, shape, f32))

        def sem(name):
            return ctx.enter_context(nc.semaphore(name))

        h_all = sb("gen_h_all", [P, B, F], f32)
        v_wide = sb("gen_v_wide", [P, N], f32)
        att = sb("gen_att", [P, N], f32)
        adj_row = sb("gen_adj_row", [P, N], i32)
        x_tile = sb("gen_x_tile", [P, F], f32)
        prop = sb("gen_prop", [P, F], f32)
        block_in = sb("gen_block_in", [P, P], f32)
        block_t = sb("gen_block_t", [P, P], f32)
        identity = sb("gen_identity", [P, P], f32)
        w_wide = sb("gen_w_wide", [HID, P], f32)
        w1_sb = sb("gen_w1", [HID, F], f32)
        w2_sb = sb("gen_w2", [HID, F], f32)
        w_col = sb("gen_w_col", [HID, 1], f32)
        b1_col = sb("gen_b1_col", [HID, 1], f32)
        bw_col = sb("gen_bw_col", [P, 1], f32)
        a1 = sb("gen_a1", [P, F], f32)
        a2 = sb("gen_a2", [P, F], f32)
        u_const = sb("gen_u_const", [P, 1], f32)
        dump = sb("gen_dump", [P, F], f32)
        big = sb("gen_big", [P, 1], f32)
        power = sb("gen_power", [P, 1], f32)
        stats = sb("gen_stats", [P, 6], f32)
        mean_var = sb("gen_mean_var", [P, 2], f32)
        rstd = sb("gen_rstd", [P, 1], f32)
        u_all = sb("gen_u_all", [P, B], f32)
        v_all = sb("gen_v_all", [P, B], f32)
        count = sb("gen_count", [P, 1], f32)
        neg_max = sb("gen_neg_max", [P, 1], f32)
        total = sb("gen_total", [P, 1], f32)
        has = sb("gen_has", [P, 1], f32)
        prop_scale = sb("gen_prop_scale", [P, 1], f32)
        h_scale = sb("gen_h_scale", [P, 1], f32)
        ps_a1, ps_a2, ps_c = pb("gen_ps_a1", [P, F]), pb("gen_ps_a2", [P, F]), pb("gen_ps_c", [P, 1])
        ps_t, ps_o = pb("gen_ps_t", [P, P]), pb("gen_ps_o", [P, F])

        loaded = sem("gen_loaded")
        dve_setup = sem("gen_dve_setup")
        w_wide_ready = sem("gen_w_wide_ready")
        weights_in_psum = sem("gen_weights_in_psum")
        identity_ready = sem("gen_identity_ready")
        identity_cleared = sem("gen_identity_cleared")
        power_ready = sem("gen_power_ready")
        wait_passed = sem("gen_wait_passed")
        dve_norm = sem("gen_dve_norm")
        var_ready = sem("gen_var_ready")
        rstd_ready = sem("gen_rstd_ready")
        v_ready = sem("gen_v_ready")
        v_stored = sem("gen_v_stored")
        v_wide_loaded = sem("gen_v_wide_loaded")
        adj_loaded = sem("gen_adj_loaded")
        x_loaded = sem("gen_x_loaded")
        dve_rows = sem("gen_dve_rows")
        logits_ready = sem("gen_logits_ready")
        exp_ready = sem("gen_exp_ready")
        block_ready = sem("gen_block_ready")
        block_turned = sem("gen_block_turned")
        block_t_ready = sem("gen_block_t_ready")
        block_done = sem("gen_block_done")
        out_ready = sem("gen_out_ready")
        out_stored = sem("gen_out_stored")

        block = ctx.enter_context(nc.Block())

        @block.sync
        def _(sp):
            sp.dma_start(w_col[:, :], ww.rearrange("o h -> h o")).then_inc(loaded, 16)
            sp.dma_start(b1_col[:, :], b1).then_inc(loaded, 16)
            sp.dma_start(bw_col[:, :], bw.to_broadcast([P, 1])).then_inc(loaded, 16)
            sp.dma_start(w1_sb[:, :], w1).then_inc(loaded, 16)
            sp.dma_start(w2_sb[:, :], w2).then_inc(loaded, 16)
            sp.dma_start(h_all[:, :, :], x_tiles).then_inc(loaded, 16)
            sp.wait_ge(v_ready, B)
            sp.dma_start(v_row.rearrange("o (b p) -> p (o b)", p=P), v_all[:, :],
                         allow_slow_non_contiguous=True).then_inc(v_stored, 16)
            sp.wait_ge(v_stored, 16)
            sp.dma_start(v_wide[:, :], v_row.to_broadcast([P, N])).then_inc(v_wide_loaded, 16)
            with sp.Fori(0, B) as b:
                sp.wait_ge(out_stored, b * 16)
                sp.dma_start(adj_row[:, :], adj_tiles[:, bass.ds(b, 1), :]).then_inc(adj_loaded, 16)
                sp.dma_start(x_tile[:, :], x_tiles[:, bass.ds(b, 1), :]).then_inc(x_loaded, 16)
                sp.wait_ge(out_ready, b + 1)
                sp.dma_start(out_tiles[:, bass.ds(b, 1), :], x_tile[:, :]).then_inc(out_stored, 16)
            sp.wait_ge(out_stored, B * 16)

        @block.gpsimd
        def _(pool):
            pool.memset(identity[:, :], 0.0).then_inc(identity_cleared, 1)
            pool.wait_ge(identity_cleared, 1)
            pool.affine_select(out=identity[:, :], in_=identity[:, :], compare_op=ALU.not_equal, fill=1.0,
                               base=0, pattern=[[-1, P]], channel_multiplier=1).then_inc(identity_ready, 1)
            pool.memset(power[:, :], -0.5).then_inc(power_ready, 1)
            pool.wait_ge(power_ready, 1)
            with pool.Fori(0, B) as b:
                pool.wait_ge(var_ready, b + 1)
                pool.tensor_tensor(rstd[:, :], mean_var[:, 1:2], power[:, :], ALU.pow).then_inc(rstd_ready, 1)

        @block.vector
        def _(dve):
            dve.memset(w_wide[:, :], 1.0).then_inc(dve_setup, 1)
            dve.memset(big[:, :], NEG_BIG).then_inc(dve_setup, 1)
            dve.wait_ge(loaded, 96)
            dve.wait_ge(dve_setup, 2)
            dve.tensor_scalar(w_wide[:, :], w_wide[:, :], w_col[:, 0:1], None, ALU.mult).then_inc(w_wide_ready, 1)
            dve.wait_ge(weights_in_psum, 3)
            dve.tensor_copy(a1[:, :], ps_a1[:, :]).then_inc(dve_setup, 1)
            dve.tensor_copy(a2[:, :], ps_a2[:, :]).then_inc(dve_setup, 1)
            dve.tensor_tensor(u_const[:, :], ps_c[:, :], bw_col[:, :], ALU.add).then_inc(dve_setup, 1)
            dve.wait_ge(dve_setup, 5)
            STEPS = 8
            with dve.Fori(0, B) as b:
                row = h_all[:, bass.ds(b, 1), :].rearrange("p o f -> p (o f)")
                dve.bn_stats(stats[:, :], row).then_inc(dve_norm, 1)
                dve.wait_ge(dve_norm, b * STEPS + 1)
                dve.sem_inc(wait_passed, 1)
                dve.bn_aggr(mean_var[:, :], stats[:, :]).then_inc(dve_norm, 1)
                dve.wait_ge(dve_norm, b * STEPS + 2)
                dve.tensor_scalar(mean_var[:, 1:2], mean_var[:, 1:2], EPS, None, ALU.add).then_inc(var_ready, 1)
                dve.wait_ge(rstd_ready, b + 1)
                dve.tensor_scalar(row, row, mean_var[:, 0:1], rstd[:, 0:1], ALU.subtract, ALU.mult).then_inc(dve_norm, 1)
                dve.wait_ge(dve_norm, b * STEPS + 3)
                dve.tensor_scalar(row, row, 0.0, None, ALU.max).then_inc(dve_norm, 1)
                dve.wait_ge(dve_norm, b * STEPS + 4)
                dve.scalar_tensor_tensor(out=dump[:, :], in0=row, scalar=1.0, in1=a1[:, :], op0=ALU.mult,
                                         op1=ALU.mult, accum_out=u_all[:, bass.ds(b, 1)]).then_inc(dve_norm, 1)
                dve.wait_ge(dve_norm, b * STEPS + 5)
                dve.tensor_tensor(u_all[:, bass.ds(b, 1)], u_all[:, bass.ds(b, 1)], u_const[:, :], ALU.add)\
                   .then_inc(dve_norm, 1)
                dve.scalar_tensor_tensor(out=dump[:, :], in0=row, scalar=1.0, in1=a2[:, :], op0=ALU.mult,
                                         op1=ALU.mult, accum_out=v_all[:, bass.ds(b, 1)]).then_inc(v_ready, 1)
                dve.wait_ge(v_ready, b + 1)
                dve.sem_inc(dve_norm, 2)
            dve.wait_ge(v_wide_loaded, 16)
            ROW_STEPS = 9
            with dve.Fori(0, B) as b:
                def step(n):
                    dve.wait_ge(dve_rows, b * ROW_STEPS + n)

                dve.wait_ge(adj_loaded, b * 16 + 16)
                dve.wait_ge(x_loaded, b * 16 + 16)
                dve.tensor_reduce(count[:, :], adj_row[:, :], AX.X, ALU.add).then_inc(dve_rows, 1)
                dve.tensor_scalar(att[:, :], v_wide[:, :], u_all[:, bass.ds(b, 1)], None, ALU.add).then_inc(dve_rows, 1)
                step(2)
                dve.tensor_scalar(adj_row[:, :], adj_row[:, :], 0.0, None, ALU.is_le).then_inc(dve_rows, 1)
                step(3)
                dve.sem_inc(wait_passed, 1)
                dve.copy_predicated(att[:, :], adj_row[:, :], big[:, 0:1].to_broadcast([P, N])).then_inc(dve_rows, 1)
                step(4)
                dve.tensor_reduce(neg_max[:, :], att[:, :], AX.X, ALU.max, negate=True).then_inc(logits_ready, 1)
                dve.wait_ge(exp_ready, b + 1)
                dve.sem_inc(wait_passed, 1)
                with dve.Fori(0, B) as j:
                    n = b * B + j
                    dve.tensor_copy(block_in[:, :], att[:, bass.ds(j * P, P)]).then_inc(block_ready, 1)
                    dve.wait_ge(block_turned, n + 1)
                    dve.tensor_copy(block_t[:, :], ps_t[:, :]).then_inc(block_t_ready, 1)
                    dve.wait_ge(block_done, n + 1)
                dve.reciprocal(prop_scale[:, :], total[:, :]).then_inc(dve_rows, 1)
                dve.tensor_scalar(has[:, :], count[:, :], 0.0, 1.0 - KEEP, ALU.is_gt, ALU.mult).then_inc(dve_rows, 1)
                step(6)
                dve.tensor_scalar(h_scale[:, :], has[:, :], -1.0, 1.0, ALU.mult, ALU.add).then_inc(dve_rows, 1)
                dve.tensor_tensor(prop_scale[:, :], prop_scale[:, :], has[:, :], ALU.mult).then_inc(dve_rows, 1)
                step(8)
                row = h_all[:, bass.ds(b, 1), :].rearrange("p o f -> p (o f)")
                dve.scalar_tensor_tensor(out=prop[:, :], in0=row, scalar=h_scale[:, 0:1], in1=x_tile[:, :],
                                         op0=ALU.mult, op1=ALU.add).then_inc(dve_rows, 1)
                step(9)
                dve.scalar_tensor_tensor(out=x_tile[:, :], in0=ps_o[:, :], scalar=prop_scale[:, 0:1], in1=prop[:, :],
                                         op0=ALU.mult, op1=ALU.add).then_inc(out_ready, 1)
                dve.wait_ge(out_ready, b + 1)

        @block.scalar
        def _(act):
            with act.Fori(0, B) as b:
                act.wait_ge(logits_ready, b + 1)
                nc.scalar.activation(att[:, :], att[:, :], ACT.Exp, bias=neg_max[:, 0:1],
                                     accum_out=total[:, 0:1]).then_inc(exp_ready, 1)

        @block.tensor
        def _(pe):
            pe.wait_ge(w_wide_ready, 1)
            nc.tensor.matmul(ps_a1[:, :], w_wide[:, :], w1_sb[:, :], start=True, stop=True).then_inc(weights_in_psum, 1)
            nc.tensor.matmul(ps_a2[:, :], w_wide[:, :], w2_sb[:, :], start=True, stop=True).then_inc(weights_in_psum, 1)
            nc.tensor.matmul(ps_c[:, :], w_wide[:, :], b1_col[:, :], start=True, stop=True).then_inc(weights_in_psum, 1)
            pe.wait_ge(identity_ready, 1)
            with pe.Fori(0, B) as b:
                def column_block(j, first, last):
                    n = b * B + j
                    pe.wait_ge(block_ready, n + 1)
                    nc.tensor.transpose(ps_t[:, :], block_in[:, :], identity[:, :]).then_inc(block_turned, 1)
                    pe.wait_ge(block_t_ready, n + 1)
                    nc.tensor.matmul(ps_o[:, :], block_t[:, :], h_all[:, bass.ds(j, 1), :].rearrange("p o f -> p (o f)"),
                                     start=first, stop=last).then_inc(block_done, 1)

                column_block(0, True, False)
                with pe.Fori(1, B - 1) as j:
                    column_block(j, False, False)
                column_block(B - 1, False, True)


def kernel(x, adj, L0_gnn_W1, L0_gnn_b1, L0_gnn_W2, L0_gnn_Ww, L0_gnn_bw):
    import numpy as np
    import concourse.bacc as bacc
    from concourse.bass_utils import run_bass_kernel_spmd

    x, adj = np.asarray(x), np.asarray(adj)
    N, F = x.shape
    T = N // P
    tiled = adj.reshape(P, T // BANKS, BANKS, P, T // PAIR, PAIR).transpose(3, 1, 4, 5, 2, 0)
    tiled = np.ascontiguousarray(tiled.transpose(1, 2, 0, 3, 4, 5)).reshape(-1, P, PAIR * BANKS * P)
    arrays = {
        "x": x, "adj": adj, "adj_tiled": tiled,
        "w1": np.asarray(L0_gnn_W1), "b1": np.asarray(L0_gnn_b1).reshape(-1, 1), "w2": np.asarray(L0_gnn_W2),
        "ww": np.asarray(L0_gnn_Ww), "bw": np.asarray(L0_gnn_bw).reshape(1, 1),
    }
    nc = bacc.Bacc("TRN2", target_bir_lowering=False, num_devices=1)
    ins = {n: nc.dram_tensor(f"in_{n}", a.shape, mybir.dt.from_np(a.dtype), kind="ExternalInput").ap()
           for n, a in arrays.items()}
    out = nc.dram_tensor("out", (N, F), mybir.dt.float32, kind="ExternalOutput").ap()
    v_row = nc.dram_tensor("v_row", (1, N), mybir.dt.float32, kind="Internal").ap()
    with nc.sbuf_tensor("flag", [1, 1], mybir.dt.int32) as flag:
        fast_program(nc, ins["x"], ins["adj_tiled"].rearrange("n p c -> p n c"), ins["w2"], ins["ww"], out, flag)
        beyond = nc.values_load(flag[0:1, 0:1], min_val=0, max_val=1)
        with nc.If(beyond > 0):
            general_program(nc, ins["x"], ins["adj"], ins["w1"], ins["b1"], ins["w2"], ins["ww"], ins["bw"], v_row, out)
        nc.end_all_ifs()
    r = run_bass_kernel_spmd(nc, [{f"in_{n}": a for n, a in arrays.items()}], core_ids=[0])
    return r.results[0]["out"]
```

```python
import concourse.bass as bass
from concourse import mybir
from contextlib import ExitStack

P = 128
EPS = 1e-5
NEG_BIG = -9000000000000000.0
KEEP = 0.5
R_MAX = 2.75
LOG_SCALE = 8.317766166719343
TINY = 1e-30
BANKS = 8
PAIR = 2
SLOTS = 4
PARTS = 2
LAST_PARTS = BANKS
WARM_UP = 10
QUAD = 4


def fast_program(nc, x, adj_tiles, w2, ww, out, flag):
    f32, f16, i32 = mybir.dt.float32, mybir.dt.float16, mybir.dt.int32
    ALU, ACT = mybir.AluOpType, mybir.ActivationFunctionType
    N, F = x.shape
    HID = w2.shape[0]
    T = N // P
    CHUNKS = T // BANKS
    BLOCKS = T // (PAIR * SLOTS)
    TURNS = CHUNKS * BLOCKS
    C = F + 1
    CP = C + 1
    assert PAIR * SLOTS == 2 * QUAD == BANKS and N % (P * BANKS) == 0 and BLOCKS >= 3

    x_tiles = x.rearrange("(p t) f -> p t f", p=P)
    out_tiles = out.rearrange("(p t) f -> p t f", p=P)

    with ExitStack() as ctx:
        def sb(name, shape, dt):
            return ctx.enter_context(nc.sbuf_tensor(name, shape, dt))

        def sem(name):
            return ctx.enter_context(nc.semaphore(name))

        adj_sb = sb("adj_sb", [P, SLOTS, PAIR * BANKS * P], i32)
        mask = sb("mask", [P, SLOTS, PAIR * BANKS * P], f16)
        mask_tiles = mask[:, :, :].rearrange("p s (t k q) -> p s t k q", t=PAIR, k=BANKS)
        g_hi = sb("g_hi", [P, T, CP], f16)
        g_lo = sb("g_lo", [P, T, CP], f16)
        x_all = sb("x_all", [P, T, F], f32)
        h1 = sb("h1", [P, 2, QUAD, CP], f32)
        x_prop = sb("x_prop", [P, BANKS, F], f32)
        h_rows = sb("h_rows", [P, BANKS, F], f32)
        w2_sb = sb("w2_sb", [HID, F], f32)
        w_col = sb("w_col", [HID, 1], f32)
        w_wide = sb("w_wide", [HID, P], f32)
        a2 = sb("a2", [P, F], f32)
        norm2 = sb("norm2", [P, 1], f32)
        r_squared = sb("r_squared", [P, 1], f32)
        bound = sb("bound", [P, 1], f32)
        exp_bias = sb("exp_bias", [P, 1], f32)
        half_power = sb("half_power", [P, 1], f32)
        neg_half_power = sb("neg_half_power", [P, QUAD], f32)
        minus_one = sb("minus_one", [P, QUAD], f32)
        stats = sb("stats", [P, 2, QUAD, 6], f32)
        mean_var = sb("mean_var", [P, 2, QUAD, 2], f32)
        var_eps = sb("var_eps", [P, 2, QUAD], f32)
        neg_mean = sb("neg_mean", [P, 2, QUAD], f32)
        rstd = sb("rstd", [P, T], f32)
        shift = sb("shift", [P, T], f32)
        v = sb("v", [P, 2, QUAD], f32)
        e = sb("e", [P, 2, QUAD], f32)
        floor_den = sb("floor_den", [P, BANKS], f32)
        prop_scale = sb("prop_scale", [P, BANKS], f32)
        h_factor = sb("h_factor", [P, BANKS], f32)
        ps = ctx.enter_context(nc.psum_tensor("ps", [P, BANKS, 512], f32))

        w_loaded = sem("w_loaded")
        w2_loaded = sem("w2_loaded")
        x_full = [sem("x_full_even"), sem("x_full_odd")]
        adj_full = [sem(f"adj_full{i}") for i in range(SLOTS)]
        mask_ready = sem("mask_ready")
        mask_free = sem("mask_free")
        w_cleared = sem("w_cleared")
        w_wide_ready = sem("w_wide_ready")
        a2_in_psum = sem("a2_in_psum")
        a2_ready = sem("a2_ready")
        norm2_ready = sem("norm2_ready")
        r_squared_ready = sem("r_squared_ready")
        flag_ready = sem("flag_ready")
        powers_ready = sem("powers_ready")
        bound_ready = sem("bound_ready")
        exp_bias_ready = sem("exp_bias_ready")
        table_loaded = sem("table_loaded")
        ones_ready = sem("ones_ready")
        bn_stats_done = sem("bn_stats_done")
        wait_passed = sem("wait_passed")
        mean_var_done = sem("mean_var_done")
        var_eps_ready = sem("var_eps_ready")
        neg_mean_ready = sem("neg_mean_ready")
        rstd_ready = sem("rstd_ready")
        shift_ready = sem("shift_ready")
        h_ready = sem("h_ready")
        v_ready = sem("v_ready")
        e_ready = sem("e_ready")
        g_hi_ready = sem("g_hi_ready")
        g_ready = sem("g_ready")
        acc_done = sem("acc_done")
        bank_read = sem("bank_read")
        den_ready = sem("den_ready")
        prop_scale_ready = sem("prop_scale_ready")
        h_factor_ready = sem("h_factor_ready")
        h_rows_ready = sem("h_rows_ready")
        out_ready = sem("out_ready")
        out_stored = [sem(f"out_stored{i}") for i in range(LAST_PARTS)]

        block = ctx.enter_context(nc.Block())

        @block.sync
        def _(sp):
            def load_adjacency(turn, slot):
                n = turn * SLOTS + slot
                sp.dma_start(adj_sb[:, slot, :], adj_tiles[:, bass.ds(n, 1), :]).then_inc(adj_full[slot], 16)

            sp.dma_start(w_col[:, :], ww.rearrange("o h -> h o")).then_inc(w_loaded, 16)
            sp.dma_start(w2_sb[:, :], w2).then_inc(w2_loaded, 16)
            for slot in range(SLOTS):
                if slot in (1, 2):
                    sp.wait_ge(x_full[slot - 1], 16)
                load_adjacency(0, slot)
            sp.dma_start(x_all[:, 3 * QUAD:4 * QUAD, :], x_tiles[:, 3 * QUAD:4 * QUAD, :]).then_inc(x_full[1], 16)
            with sp.Fori(1, TURNS) as turn:
                for slot in range(SLOTS):
                    sp.wait_ge(mask_ready, turn * SLOTS + slot - (SLOTS - 1))
                    load_adjacency(turn, slot)

        @block.gpsimd
        def _(pool):
            pool.memset(neg_half_power[:, :], -0.5).then_inc(powers_ready, 1)
            pool.memset(half_power[:, :], 0.5).then_inc(powers_ready, 1)
            pool.memset(minus_one[:, :], -1.0).then_inc(powers_ready, 1)
            pool.wait_ge(powers_ready, 3)

            def normalisers(quad, half):
                own = bass.ds(quad * QUAD, QUAD)
                pool.wait_ge(mean_var_done, quad * QUAD + QUAD)
                pool.tensor_tensor(neg_mean[:, half, :], mean_var[:, half, :, 0], minus_one[:, :], ALU.mult)\
                    .then_inc(neg_mean_ready, 1)
                pool.tensor_scalar(var_eps[:, half, :], mean_var[:, half, :, 1], EPS, 4.0, ALU.add, ALU.mult)\
                    .then_inc(var_eps_ready, 1)
                pool.wait_ge(var_eps_ready, quad + 1)
                pool.tensor_tensor(rstd[:, own], var_eps[:, half, :], neg_half_power[:, :], ALU.pow).then_inc(rstd_ready, 1)
                pool.wait_ge(neg_mean_ready, quad + 1)
                pool.wait_ge(rstd_ready, quad + 1)
                pool.tensor_tensor(shift[:, own], neg_mean[:, half, :], rstd[:, own], ALU.mult).then_inc(shift_ready, 1)

            normalisers(0, 0)
            pool.wait_ge(r_squared_ready, 1)
            pool.tensor_tensor(bound[:, :], r_squared[:, :], half_power[:, :], ALU.pow).then_inc(bound_ready, 1)
            pool.wait_ge(bound_ready, 1)
            pool.tensor_scalar(exp_bias[:, :], bound[:, :], -1.0, LOG_SCALE, ALU.mult, ALU.add).then_inc(exp_bias_ready, 1)
            normalisers(1, 1)
            with pool.Fori(1, BLOCKS) as blk:
                for half in range(2):
                    normalisers(blk * 2 + half, half)

        @block.vector
        def _(dve):
            def statistics(quad, half):
                dve.wait_ge(x_full[half], (quad - half) * 8 + 16)
                for t in range(QUAD):
                    row = x_all[:, bass.ds(quad * QUAD + t, 1), :].rearrange("p o f -> p (o f)")
                    dve.bn_stats(stats[:, half, t, :], row).then_inc(bn_stats_done, 1)
                dve.wait_ge(bn_stats_done, quad * QUAD + QUAD)
                dve.sem_inc(wait_passed, 1)
                for t in range(QUAD):
                    dve.bn_aggr(mean_var[:, half, t, :], stats[:, half, t, :]).then_inc(mean_var_done, 1)

            def make_mask(turn, slot):
                dve.wait_ge(adj_full[slot], turn * 16 + 16)
                dve.wait_ge(mask_free, turn * SLOTS + slot + 1)
                dve.tensor_scalar(mask[:, slot, :], adj_sb[:, slot, :], 0.0, None, ALU.is_gt)\
                   .then_inc(mask_ready, 1)

            def logits(quad, half):
                for t in range(QUAD):
                    dve.wait_ge(h_ready, quad * QUAD + t + 1)
                    dve.scalar_tensor_tensor(out=h_rows[:, half * QUAD + t, :], in0=h1[:, half, t, 0:F], scalar=1.0,
                                             in1=a2[:, :], op0=ALU.mult, op1=ALU.mult, accum_out=v[:, half, t:t + 1])\
                       .then_inc(v_ready, 1)

            def low_parts(quad, half):
                for t in range(QUAD):
                    dve.wait_ge(g_hi_ready, quad * QUAD + t + 1)
                    own = bass.ds(quad * QUAD + t, 1)
                    dve.scalar_tensor_tensor(
                        out=g_lo[:, own, 0:C].rearrange("p o c -> p (o c)"), in0=h1[:, half, t, 0:C],
                        scalar=e[:, half, t:t + 1], in1=g_hi[:, own, 0:C].rearrange("p o c -> p (o c)"),
                        op0=ALU.mult, op1=ALU.subtract).then_inc(g_ready, 1)

            def first_chunk(blk, half, more):
                quad = blk * 2 + half
                if more:
                    statistics(quad + 1, 1 - half)
                logits(quad, half)
                make_mask(blk, 2 * half)
                make_mask(blk, 2 * half + 1)
                low_parts(quad, half)

            def finish_rows(chunk, last):
                parts = LAST_PARTS if last else PARTS
                size = BANKS // parts

                def take_sums(part):
                    n = chunk * PARTS + part + 1
                    banks = slice(part * size, part * size + size)
                    if last or part < parts - 1:
                        dve.wait_ge(acc_done, chunk * (BANKS - 1) + (part + 1) * size)
                    else:
                        dve.wait_ge(mask_free, (chunk + 1) * (BLOCKS * SLOTS) + SLOTS)
                    dve.tensor_scalar(floor_den[:, banks], ps[:, banks, F], TINY, None, ALU.max).then_inc(den_ready, 1)
                    dve.tensor_scalar(h_factor[:, banks], ps[:, banks, F], 0.0, 1.0, ALU.is_le, ALU.add)\
                       .then_inc(h_factor_ready, 1)
                    dve.wait_ge(den_ready, n)
                    dve.reciprocal(prop_scale[:, banks], floor_den[:, banks]).then_inc(prop_scale_ready, 1)
                    dve.wait_ge(prop_scale_ready, n)
                    for k in range(part * size, part * size + size):
                        row = x_all[:, bass.ds(chunk * BANKS + k, 1), :].rearrange("p o f -> p (o f)")
                        dve.scalar_tensor_tensor(out=x_prop[:, k, :], in0=ps[:, k, 0:F], scalar=prop_scale[:, k:k + 1],
                                                 in1=row, op0=ALU.mult, op1=ALU.add).then_inc(bank_read, 1)

                def add_h(part):
                    dve.wait_ge(h_factor_ready, chunk * PARTS + part + 1)
                    dve.wait_ge(bank_read, chunk * BANKS + (part + 1) * size + BANKS)
                    for k in range(part * size, part * size + size):
                        dve.scalar_tensor_tensor(out=x_prop[:, k, :], in0=h_rows[:, k, :], scalar=h_factor[:, k:k + 1],
                                                 in1=x_prop[:, k, :], op0=ALU.mult, op1=ALU.add).then_inc(out_ready, 1)

                dve.wait_ge(h_rows_ready, chunk * BANKS + BANKS)
                if last:
                    for part in range(parts):
                        take_sums(part)
                        add_h(part)
                else:
                    for part in range(parts):
                        take_sums(part)
                    for part in range(parts):
                        add_h(part)

            dve.memset(w_wide[:, :], 1.0).then_inc(w_cleared, 1)
            dve.memset(h1[:, :, :, F:CP], 1.0).then_inc(ones_ready, 1)
            dve.wait_ge(w_loaded, 16)
            dve.wait_ge(w_cleared, 1)
            dve.tensor_scalar(w_wide[:, :], w_wide[:, :], w_col[:, 0:1], None, ALU.mult).then_inc(w_wide_ready, 1)
            statistics(0, 0)
            dve.wait_ge(a2_in_psum, 1)
            dve.tensor_scalar(a2[:, :], ps[:, 0, 0:F], 2.0, None, ALU.mult).then_inc(a2_ready, 1)
            dve.wait_ge(a2_ready, 1)
            dve.sem_inc(bank_read, BANKS)
            dve.scalar_tensor_tensor(out=x_prop[:, 0, :], in0=a2[:, :], scalar=1.0, in1=a2[:, :], op0=ALU.mult,
                                     op1=ALU.mult, accum_out=norm2[:, 0:1]).then_inc(norm2_ready, 1)
            dve.wait_ge(norm2_ready, 1)
            dve.tensor_scalar(r_squared[:, :], norm2[:, :], F / 4.0, None, ALU.mult).then_inc(r_squared_ready, 1)
            dve.tensor_scalar(flag[0:1, 0:1], norm2[0:1, :], 4.0 * R_MAX * R_MAX / F, None, ALU.is_gt)\
               .then_inc(flag_ready, 1)

            statistics(1, 1)
            logits(0, 0)
            make_mask(0, 0)
            low_parts(0, 0)
            make_mask(0, 1)
            first_chunk(0, 1, True)
            with dve.Fori(1, BLOCKS - 1) as blk:
                first_chunk(blk, 0, True)
                first_chunk(blk, 1, True)
            first_chunk(BLOCKS - 1, 0, True)
            first_chunk(BLOCKS - 1, 1, False)
            with dve.Fori(1, CHUNKS) as chunk:
                for slot in range(SLOTS - 1):
                    make_mask(chunk * BLOCKS, slot)
                finish_rows(chunk - 1, False)
                make_mask(chunk * BLOCKS, SLOTS - 1)
                with dve.Fori(1, BLOCKS) as blk:
                    for slot in range(SLOTS):
                        make_mask(chunk * BLOCKS + blk, slot)
            finish_rows(CHUNKS - 1, True)

        @block.scalar
        def _(act):
            def load_x(quad, half):
                act.dma_start(x_all[:, bass.ds(quad * QUAD, QUAD), :], x_tiles[:, bass.ds(quad * QUAD, QUAD), :])\
                   .then_inc(x_full[half], 16)

            def make_g(blk, more):
                for half in range(2):
                    quad = blk * 2 + half
                    act.wait_ge(shift_ready, quad + 1)
                    for t in range(QUAD):
                        at = quad * QUAD + t
                        row = x_all[:, bass.ds(at, 1), :].rearrange("p o f -> p (o f)")
                        nc.scalar.activation(h1[:, half, t, 0:F], row, ACT.Relu, bias=shift[:, bass.ds(at, 1)],
                                             scale=rstd[:, bass.ds(at, 1)]).then_inc(h_ready, 1)
                    act.wait_ge(exp_bias_ready, 1)
                    act.wait_ge(v_ready, quad * QUAD + QUAD)
                    nc.scalar.activation(e[:, half, :], v[:, half, :], ACT.Exp, bias=exp_bias[:, 0:1]).then_inc(e_ready, 1)
                    act.wait_ge(ones_ready, 1)
                    act.wait_ge(e_ready, quad + 1)
                    act.wait_ge(h_ready, quad * QUAD + QUAD)
                    for t in range(QUAD):
                        own = bass.ds(quad * QUAD + t, 1)
                        nc.scalar.activation(g_hi[:, own, 0:C].rearrange("p o c -> p (o c)"), h1[:, half, t, 0:C],
                                             ACT.Copy, scale=e[:, half, t:t + 1]).then_inc(g_hi_ready, 1)
                    if more:
                        act.wait_ge(x_full[half], blk * 16 + 32)
                        load_x(quad + 4, half)

            def h_terms(chunk, parts):
                for k in range(BANKS):
                    at = chunk * BANKS + k
                    row = x_all[:, bass.ds(at, 1), :].rearrange("p o f -> p (o f)")
                    nc.scalar.activation(h_rows[:, k, :], row, ACT.Relu, bias=shift[:, bass.ds(at, 1)],
                                         scale=rstd[:, bass.ds(at, 1)]).then_inc(h_rows_ready, 1)
                size = BANKS // parts
                for part in range(parts):
                    act.wait_ge(out_ready, chunk * BANKS + part * size + size)
                    act.dma_start(out_tiles[:, bass.ds(chunk * BANKS + part * size, size), :],
                                  x_prop[:, part * size:part * size + size, :]).then_inc(out_stored[part], 16)
                for part in range(parts):
                    act.wait_ge(out_stored[part], chunk * 16 + 16 if part < PARTS else 16)

            load_x(0, 0)
            load_x(1, 1)
            act.wait_ge(powers_ready, 1)
            nc.scalar.activation(e[:, 0, :], neg_half_power[:, :], ACT.Exp).then_inc(table_loaded, 1)
            act.wait_ge(table_loaded, 1)
            act.wait_ge(x_full[0], 16)
            load_x(2, 0)
            with act.Fori(0, BLOCKS - 2) as blk:
                make_g(blk, True)
            make_g(BLOCKS - 2, False)
            make_g(BLOCKS - 1, False)
            with act.Fori(0, CHUNKS - 1) as chunk:
                h_terms(chunk, PARTS)
            h_terms(CHUNKS - 1, LAST_PARTS)
            act.wait_ge(flag_ready, 1)

        @block.tensor
        def _(pe):
            def times_g(k, blk, slot, t, begins, ends):
                tile = bass.ds(blk * (SLOTS * PAIR) + slot * PAIR + t, 1)
                nc.tensor.matmul(ps[:, k, 0:C], mask_tiles[:, slot, t, k, :],
                                 g_hi[:, tile, 0:C].rearrange("p o c -> p (o c)"), start=begins, stop=False)
                return nc.tensor.matmul(ps[:, k, 0:C], mask_tiles[:, slot, t, k, :],
                                        g_lo[:, tile, 0:C].rearrange("p o c -> p (o c)"), start=False, stop=ends)

            def product(chunk, blk, first=False, last=False):
                for slot in range(SLOTS):
                    pe.wait_ge(mask_ready, (chunk * BLOCKS + blk) * SLOTS + slot + 1)
                    pe.wait_ge(g_ready, (blk * SLOTS + slot + 1) * PAIR)
                    for k in range(BANKS):
                        if first and slot == 0:
                            pe.wait_ge(bank_read, chunk * BANKS + k + 1)
                        for t in range(PAIR):
                            ends = last and slot == SLOTS - 1 and t == PAIR - 1
                            done = times_g(k, blk, slot, t, first and slot == 0 and t == 0, ends)
                            if k == BANKS - 1 and t == PAIR - 1:
                                done.then_inc(mask_free, 1)
                            elif ends:
                                done.then_inc(acc_done, 1)

            def last_product(chunk, blk):
                for k in range(BANKS):
                    for slot in range(SLOTS):
                        if k == 0:
                            pe.wait_ge(mask_ready, (chunk * BLOCKS + blk) * SLOTS + slot + 1)
                        for t in range(PAIR):
                            ends = slot == SLOTS - 1 and t == PAIR - 1
                            done = times_g(k, blk, slot, t, False, ends)
                    done.then_inc(acc_done, 1)

            pe.sem_inc(mask_free, SLOTS)
            pe.wait_ge(w_wide_ready, 1)
            pe.wait_ge(w2_loaded, 16)
            nc.tensor.matmul(ps[:, 0, 0:F], w_wide[:, :], w2_sb[:, :], start=True, stop=True).then_inc(a2_in_psum, 1)
            for _ in range(WARM_UP):
                nc.tensor.matmul(ps[:, BANKS - 1, 0:F], w_wide[:, :], w2_sb[:, :], start=True, stop=True)
            with pe.Fori(0, CHUNKS - 1) as chunk:
                product(chunk, 0, first=True)
                with pe.Fori(1, BLOCKS - 1) as blk:
                    product(chunk, blk)
                product(chunk, BLOCKS - 1, last=True)
            product(CHUNKS - 1, 0, first=True)
            with pe.Fori(1, BLOCKS - 1) as blk:
                product(CHUNKS - 1, blk)
            last_product(CHUNKS - 1, BLOCKS - 1)


def general_program(nc, x, adj, w1, b1, w2, ww, bw, v_row, out):
    f32, i32 = mybir.dt.float32, mybir.dt.int32
    ALU, ACT, AX = mybir.AluOpType, mybir.ActivationFunctionType, mybir.AxisListType
    N, F = x.shape
    HID = w2.shape[0]
    B = N // P

    x_tiles = x.rearrange("(b p) f -> p b f", p=P)
    out_tiles = out.rearrange("(b p) f -> p b f", p=P)
    adj_tiles = adj.rearrange("(b p) n -> p b n", p=P)

    with ExitStack() as ctx:
        def sb(name, shape, dt):
            return ctx.enter_context(nc.sbuf_tensor(name, shape, dt))

        def pb(name, shape):
            return ctx.enter_context(nc.psum_tensor(name, shape, f32))

        def sem(name):
            return ctx.enter_context(nc.semaphore(name))

        h_all = sb("gen_h_all", [P, B, F], f32)
        v_wide = sb("gen_v_wide", [P, N], f32)
        att = sb("gen_att", [P, N], f32)
        adj_row = sb("gen_adj_row", [P, N], i32)
        x_tile = sb("gen_x_tile", [P, F], f32)
        prop = sb("gen_prop", [P, F], f32)
        block_in = sb("gen_block_in", [P, P], f32)
        block_t = sb("gen_block_t", [P, P], f32)
        identity = sb("gen_identity", [P, P], f32)
        w_wide = sb("gen_w_wide", [HID, P], f32)
        w1_sb = sb("gen_w1", [HID, F], f32)
        w2_sb = sb("gen_w2", [HID, F], f32)
        w_col = sb("gen_w_col", [HID, 1], f32)
        b1_col = sb("gen_b1_col", [HID, 1], f32)
        bw_col = sb("gen_bw_col", [P, 1], f32)
        a1 = sb("gen_a1", [P, F], f32)
        a2 = sb("gen_a2", [P, F], f32)
        u_const = sb("gen_u_const", [P, 1], f32)
        dump = sb("gen_dump", [P, F], f32)
        big = sb("gen_big", [P, 1], f32)
        power = sb("gen_power", [P, 1], f32)
        stats = sb("gen_stats", [P, 6], f32)
        mean_var = sb("gen_mean_var", [P, 2], f32)
        rstd = sb("gen_rstd", [P, 1], f32)
        u_all = sb("gen_u_all", [P, B], f32)
        v_all = sb("gen_v_all", [P, B], f32)
        count = sb("gen_count", [P, 1], f32)
        neg_max = sb("gen_neg_max", [P, 1], f32)
        total = sb("gen_total", [P, 1], f32)
        has = sb("gen_has", [P, 1], f32)
        prop_scale = sb("gen_prop_scale", [P, 1], f32)
        h_scale = sb("gen_h_scale", [P, 1], f32)
        ps_a1, ps_a2, ps_c = pb("gen_ps_a1", [P, F]), pb("gen_ps_a2", [P, F]), pb("gen_ps_c", [P, 1])
        ps_t, ps_o = pb("gen_ps_t", [P, P]), pb("gen_ps_o", [P, F])

        loaded = sem("gen_loaded")
        dve_setup = sem("gen_dve_setup")
        w_wide_ready = sem("gen_w_wide_ready")
        weights_in_psum = sem("gen_weights_in_psum")
        identity_ready = sem("gen_identity_ready")
        identity_cleared = sem("gen_identity_cleared")
        power_ready = sem("gen_power_ready")
        wait_passed = sem("gen_wait_passed")
        dve_norm = sem("gen_dve_norm")
        var_ready = sem("gen_var_ready")
        rstd_ready = sem("gen_rstd_ready")
        v_ready = sem("gen_v_ready")
        v_stored = sem("gen_v_stored")
        v_wide_loaded = sem("gen_v_wide_loaded")
        adj_loaded = sem("gen_adj_loaded")
        x_loaded = sem("gen_x_loaded")
        dve_rows = sem("gen_dve_rows")
        logits_ready = sem("gen_logits_ready")
        exp_ready = sem("gen_exp_ready")
        block_ready = sem("gen_block_ready")
        block_turned = sem("gen_block_turned")
        block_t_ready = sem("gen_block_t_ready")
        block_done = sem("gen_block_done")
        out_ready = sem("gen_out_ready")
        out_stored = sem("gen_out_stored")

        block = ctx.enter_context(nc.Block())

        @block.sync
        def _(sp):
            sp.dma_start(w_col[:, :], ww.rearrange("o h -> h o")).then_inc(loaded, 16)
            sp.dma_start(b1_col[:, :], b1).then_inc(loaded, 16)
            sp.dma_start(bw_col[:, :], bw.to_broadcast([P, 1])).then_inc(loaded, 16)
            sp.dma_start(w1_sb[:, :], w1).then_inc(loaded, 16)
            sp.dma_start(w2_sb[:, :], w2).then_inc(loaded, 16)
            sp.dma_start(h_all[:, :, :], x_tiles).then_inc(loaded, 16)
            sp.wait_ge(v_ready, B)
            sp.dma_start(v_row.rearrange("o (b p) -> p (o b)", p=P), v_all[:, :],
                         allow_slow_non_contiguous=True).then_inc(v_stored, 16)
            sp.wait_ge(v_stored, 16)
            sp.dma_start(v_wide[:, :], v_row.to_broadcast([P, N])).then_inc(v_wide_loaded, 16)
            with sp.Fori(0, B) as b:
                sp.dma_start(adj_row[:, :], adj_tiles[:, bass.ds(b, 1), :]).then_inc(adj_loaded, 16)
                sp.dma_start(x_tile[:, :], x_tiles[:, bass.ds(b, 1), :]).then_inc(x_loaded, 16)
                sp.wait_ge(out_ready, b + 1)
                sp.dma_start(out_tiles[:, bass.ds(b, 1), :], x_tile[:, :]).then_inc(out_stored, 16)
                sp.wait_ge(out_stored, b * 16 + 16)
                sp.sem_inc(wait_passed, 1)

        @block.gpsimd
        def _(pool):
            pool.memset(identity[:, :], 0.0).then_inc(identity_cleared, 1)
            pool.wait_ge(identity_cleared, 1)
            pool.affine_select(out=identity[:, :], in_=identity[:, :], compare_op=ALU.not_equal, fill=1.0,
                               base=0, pattern=[[-1, P]], channel_multiplier=1).then_inc(identity_ready, 1)
            pool.memset(power[:, :], -0.5).then_inc(power_ready, 1)
            pool.wait_ge(power_ready, 1)
            with pool.Fori(0, B) as b:
                pool.wait_ge(var_ready, b + 1)
                pool.tensor_tensor(rstd[:, :], mean_var[:, 1:2], power[:, :], ALU.pow).then_inc(rstd_ready, 1)

        @block.vector
        def _(dve):
            dve.memset(w_wide[:, :], 1.0).then_inc(dve_setup, 1)
            dve.memset(big[:, :], NEG_BIG).then_inc(dve_setup, 1)
            dve.wait_ge(loaded, 96)
            dve.wait_ge(dve_setup, 2)
            dve.tensor_scalar(w_wide[:, :], w_wide[:, :], w_col[:, 0:1], None, ALU.mult).then_inc(w_wide_ready, 1)
            dve.wait_ge(weights_in_psum, 3)
            dve.tensor_copy(a1[:, :], ps_a1[:, :]).then_inc(dve_setup, 1)
            dve.tensor_copy(a2[:, :], ps_a2[:, :]).then_inc(dve_setup, 1)
            dve.tensor_tensor(u_const[:, :], ps_c[:, :], bw_col[:, :], ALU.add).then_inc(dve_setup, 1)
            dve.wait_ge(dve_setup, 5)
            STEPS = 8
            with dve.Fori(0, B) as b:
                row = h_all[:, bass.ds(b, 1), :].rearrange("p o f -> p (o f)")
                dve.bn_stats(stats[:, :], row).then_inc(dve_norm, 1)
                dve.wait_ge(dve_norm, b * STEPS + 1)
                dve.sem_inc(wait_passed, 1)
                dve.bn_aggr(mean_var[:, :], stats[:, :]).then_inc(dve_norm, 1)
                dve.wait_ge(dve_norm, b * STEPS + 2)
                dve.tensor_scalar(mean_var[:, 1:2], mean_var[:, 1:2], EPS, None, ALU.add).then_inc(var_ready, 1)
                dve.wait_ge(rstd_ready, b + 1)
                dve.tensor_scalar(row, row, mean_var[:, 0:1], rstd[:, 0:1], ALU.subtract, ALU.mult).then_inc(dve_norm, 1)
                dve.wait_ge(dve_norm, b * STEPS + 3)
                dve.tensor_scalar(row, row, 0.0, None, ALU.max).then_inc(dve_norm, 1)
                dve.wait_ge(dve_norm, b * STEPS + 4)
                dve.scalar_tensor_tensor(out=dump[:, :], in0=row, scalar=1.0, in1=a1[:, :], op0=ALU.mult,
                                         op1=ALU.mult, accum_out=u_all[:, bass.ds(b, 1)]).then_inc(dve_norm, 1)
                dve.wait_ge(dve_norm, b * STEPS + 5)
                dve.tensor_tensor(u_all[:, bass.ds(b, 1)], u_all[:, bass.ds(b, 1)], u_const[:, :], ALU.add)\
                   .then_inc(dve_norm, 1)
                dve.scalar_tensor_tensor(out=dump[:, :], in0=row, scalar=1.0, in1=a2[:, :], op0=ALU.mult,
                                         op1=ALU.mult, accum_out=v_all[:, bass.ds(b, 1)]).then_inc(v_ready, 1)
                dve.wait_ge(v_ready, b + 1)
                dve.sem_inc(dve_norm, 2)
            dve.wait_ge(v_wide_loaded, 16)
            ROW_STEPS = 9
            with dve.Fori(0, B) as b:
                def step(n):
                    dve.wait_ge(dve_rows, b * ROW_STEPS + n)

                dve.wait_ge(adj_loaded, b * 16 + 16)
                dve.wait_ge(x_loaded, b * 16 + 16)
                dve.tensor_reduce(count[:, :], adj_row[:, :], AX.X, ALU.add).then_inc(dve_rows, 1)
                dve.tensor_scalar(att[:, :], v_wide[:, :], u_all[:, bass.ds(b, 1)], None, ALU.add).then_inc(dve_rows, 1)
                step(2)
                dve.tensor_scalar(adj_row[:, :], adj_row[:, :], 0.0, None, ALU.is_le).then_inc(dve_rows, 1)
                step(3)
                dve.sem_inc(wait_passed, 1)
                dve.copy_predicated(att[:, :], adj_row[:, :], big[:, 0:1].to_broadcast([P, N])).then_inc(dve_rows, 1)
                step(4)
                dve.tensor_reduce(neg_max[:, :], att[:, :], AX.X, ALU.max, negate=True).then_inc(logits_ready, 1)
                dve.wait_ge(exp_ready, b + 1)
                dve.sem_inc(wait_passed, 1)
                with dve.Fori(0, B) as j:
                    n = b * B + j
                    dve.tensor_copy(block_in[:, :], att[:, bass.ds(j * P, P)]).then_inc(block_ready, 1)
                    dve.wait_ge(block_turned, n + 1)
                    dve.tensor_copy(block_t[:, :], ps_t[:, :]).then_inc(block_t_ready, 1)
                    dve.wait_ge(block_done, n + 1)
                dve.reciprocal(prop_scale[:, :], total[:, :]).then_inc(dve_rows, 1)
                dve.tensor_scalar(has[:, :], count[:, :], 0.0, 1.0 - KEEP, ALU.is_gt, ALU.mult).then_inc(dve_rows, 1)
                step(6)
                dve.tensor_scalar(h_scale[:, :], has[:, :], -1.0, 1.0, ALU.mult, ALU.add).then_inc(dve_rows, 1)
                dve.tensor_tensor(prop_scale[:, :], prop_scale[:, :], has[:, :], ALU.mult).then_inc(dve_rows, 1)
                step(8)
                row = h_all[:, bass.ds(b, 1), :].rearrange("p o f -> p (o f)")
                dve.scalar_tensor_tensor(out=prop[:, :], in0=row, scalar=h_scale[:, 0:1], in1=x_tile[:, :],
                                         op0=ALU.mult, op1=ALU.add).then_inc(dve_rows, 1)
                step(9)
                dve.scalar_tensor_tensor(out=x_tile[:, :], in0=ps_o[:, :], scalar=prop_scale[:, 0:1], in1=prop[:, :],
                                         op0=ALU.mult, op1=ALU.add).then_inc(out_ready, 1)
                dve.wait_ge(out_ready, b + 1)

        @block.scalar
        def _(act):
            with act.Fori(0, B) as b:
                act.wait_ge(logits_ready, b + 1)
                nc.scalar.activation(att[:, :], att[:, :], ACT.Exp, bias=neg_max[:, 0:1],
                                     accum_out=total[:, 0:1]).then_inc(exp_ready, 1)

        @block.tensor
        def _(pe):
            pe.wait_ge(w_wide_ready, 1)
            nc.tensor.matmul(ps_a1[:, :], w_wide[:, :], w1_sb[:, :], start=True, stop=True).then_inc(weights_in_psum, 1)
            nc.tensor.matmul(ps_a2[:, :], w_wide[:, :], w2_sb[:, :], start=True, stop=True).then_inc(weights_in_psum, 1)
            nc.tensor.matmul(ps_c[:, :], w_wide[:, :], b1_col[:, :], start=True, stop=True).then_inc(weights_in_psum, 1)
            pe.wait_ge(identity_ready, 1)
            with pe.Fori(0, B) as b:
                def column_block(j, first, last):
                    n = b * B + j
                    pe.wait_ge(block_ready, n + 1)
                    nc.tensor.transpose(ps_t[:, :], block_in[:, :], identity[:, :]).then_inc(block_turned, 1)
                    pe.wait_ge(block_t_ready, n + 1)
                    nc.tensor.matmul(ps_o[:, :], block_t[:, :], h_all[:, bass.ds(j, 1), :].rearrange("p o f -> p (o f)"),
                                     start=first, stop=last).then_inc(block_done, 1)

                column_block(0, True, False)
                with pe.Fori(1, B - 1) as j:
                    column_block(j, False, False)
                column_block(B - 1, False, True)


def kernel(x, adj, L0_gnn_W1, L0_gnn_b1, L0_gnn_W2, L0_gnn_Ww, L0_gnn_bw):
    import numpy as np
    import concourse.bacc as bacc
    from concourse.bass_utils import run_bass_kernel_spmd

    x, adj = np.asarray(x), np.asarray(adj)
    N, F = x.shape
    T = N // P
    tiled = adj.reshape(P, T // BANKS, BANKS, P, T // PAIR, PAIR).transpose(3, 1, 4, 5, 2, 0)
    tiled = np.ascontiguousarray(tiled.transpose(1, 2, 0, 3, 4, 5)).reshape(-1, P, PAIR * BANKS * P)
    arrays = {
        "x": x, "adj": adj, "adj_tiled": tiled,
        "w1": np.asarray(L0_gnn_W1), "b1": np.asarray(L0_gnn_b1).reshape(-1, 1), "w2": np.asarray(L0_gnn_W2),
        "ww": np.asarray(L0_gnn_Ww), "bw": np.asarray(L0_gnn_bw).reshape(1, 1),
    }
    nc = bacc.Bacc("TRN2", target_bir_lowering=False, num_devices=1)
    ins = {n: nc.dram_tensor(f"in_{n}", a.shape, mybir.dt.from_np(a.dtype), kind="ExternalInput").ap()
           for n, a in arrays.items()}
    out = nc.dram_tensor("out", (N, F), mybir.dt.float32, kind="ExternalOutput").ap()
    v_row = nc.dram_tensor("v_row", (1, N), mybir.dt.float32, kind="Internal").ap()
    with nc.sbuf_tensor("flag", [1, 1], mybir.dt.int32) as flag:
        fast_program(nc, ins["x"], ins["adj_tiled"].rearrange("n p c -> p n c"), ins["w2"], ins["ww"], out, flag)
        beyond = nc.values_load(flag[0:1, 0:1], min_val=0, max_val=1)
        with nc.If(beyond > 0):
            general_program(nc, ins["x"], ins["adj"], ins["w1"], ins["b1"], ins["w2"], ins["ww"], ins["bw"], v_row, out)
        nc.end_all_ifs()
    r = run_bass_kernel_spmd(nc, [{f"in_{n}": a for n, a in arrays.items()}], core_ids=[0])
    return r.results[0]["out"]
```
